# Optimizing a Trainium2 kernel written in Bass

```python
import numpy as np
import jax
import jax.numpy as jnp

def _softmax(x, axis=-1):
    return jax.nn.softmax(x, axis=axis)

def _gelu(x):
    return jax.nn.gelu(x, approximate=True)

def _silu(x):
    return jax.nn.silu(x)

def _sigmoid(x):
    return jax.nn.sigmoid(x)

def _layernorm(x, axis=-1, eps=1e-05):
    m = jnp.mean(x, axis=axis, keepdims=True)
    v = jnp.var(x, axis=axis, keepdims=True)
    return (x - m) / jnp.sqrt(v + eps)

def _scatter_add(tgt, idx, src, axis=0):
    return tgt.at[idx].add(src)

def _segment_sum(src, seg, n):
    return jax.ops.segment_sum(src, seg, n)
kernel_name = 'mk_dlrm_tower_d1_rec_r8_6732dc'

def setup_inputs(seed: int=0):
    np.random.seed(seed)
    _w = jnp.asarray

    def _rec_inputs():
        import jax
        import jax.numpy as jnp
        _tk = jax.random.key(seed)
        ids = jnp.stack([jax.random.randint(jax.random.fold_in(_tk, 200 + f), (512,), 0, v, jnp.int32) for f, v in enumerate([1250, 1250, 1250, 12500, 125000, 1000, 1000, 1000, 1250, 12500, 1250, 1250, 1000, 1250, 1000, 1250, 1000, 1250, 1250, 12500, 1250, 1000, 1250, 1250, 1250, 1250])], axis=1)
        tbl_0 = 0.05 * jax.random.normal(jax.random.fold_in(_tk, 500 + 0), (1250, 128), jnp.float32)
        tbl_1 = 0.05 * jax.random.normal(jax.random.fold_in(_tk, 500 + 1), (1250, 128), jnp.float32)
        tbl_2 = 0.05 * jax.random.normal(jax.random.fold_in(_tk, 500 + 2), (1250, 128), jnp.float32)
        tbl_3 = 0.05 * jax.random.normal(jax.random.fold_in(_tk, 500 + 3), (12500, 128), jnp.float32)
        tbl_4 = 0.05 * jax.random.normal(jax.random.fold_in(_tk, 500 + 4), (125000, 128), jnp.float32)
        tbl_5 = 0.05 * jax.random.normal(jax.random.fold_in(_tk, 500 + 5), (1000, 128), jnp.float32)
        tbl_6 = 0.05 * jax.random.normal(jax.random.fold_in(_tk, 500 + 6), (1000, 128), jnp.float32)
        tbl_7 = 0.05 * jax.random.normal(jax.random.fold_in(_tk, 500 + 7), (1000, 128), jnp.float32)
        tbl_8 = 0.05 * jax.random.normal(jax.random.fold_in(_tk, 500 + 8), (1250, 128), jnp.float32)
        tbl_9 = 0.05 * jax.random.normal(jax.random.fold_in(_tk, 500 + 9), (12500, 128), jnp.float32)
        tbl_10 = 0.05 * jax.random.normal(jax.random.fold_in(_tk, 500 + 10), (1250, 128), jnp.float32)
        tbl_11 = 0.05 * jax.random.normal(jax.random.fold_in(_tk, 500 + 11), (1250, 128), jnp.float32)
        tbl_12 = 0.05 * jax.random.normal(jax.random.fold_in(_tk, 500 + 12), (1000, 128), jnp.float32)
        tbl_13 = 0.05 * jax.random.normal(jax.random.fold_in(_tk, 500 + 13), (1250, 128), jnp.float32)
        tbl_14 = 0.05 * jax.random.normal(jax.random.fold_in(_tk, 500 + 14), (1000, 128), jnp.float32)
        tbl_15 = 0.05 * jax.random.normal(jax.random.fold_in(_tk, 500 + 15), (1250, 128), jnp.float32)
        tbl_16 = 0.05 * jax.random.normal(jax.random.fold_in(_tk, 500 + 16), (1000, 128), jnp.float32)
        tbl_17 = 0.05 * jax.random.normal(jax.random.fold_in(_tk, 500 + 17), (1250, 128), jnp.float32)
        tbl_18 = 0.05 * jax.random.normal(jax.random.fold_in(_tk, 500 + 18), (1250, 128), jnp.float32)
        tbl_19 = 0.05 * jax.random.normal(jax.random.fold_in(_tk, 500 + 19), (12500, 128), jnp.float32)
        tbl_20 = 0.05 * jax.random.normal(jax.random.fold_in(_tk, 500 + 20), (1250, 128), jnp.float32)
        tbl_21 = 0.05 * jax.random.normal(jax.random.fold_in(_tk, 500 + 21), (1000, 128), jnp.float32)
        tbl_22 = 0.05 * jax.random.normal(jax.random.fold_in(_tk, 500 + 22), (1250, 128), jnp.float32)
        tbl_23 = 0.05 * jax.random.normal(jax.random.fold_in(_tk, 500 + 23), (1250, 128), jnp.float32)
        tbl_24 = 0.05 * jax.random.normal(jax.random.fold_in(_tk, 500 + 24), (1250, 128), jnp.float32)
        tbl_25 = 0.05 * jax.random.normal(jax.random.fold_in(_tk, 500 + 25), (1250, 128), jnp.float32)
        _rk = jax.random.fold_in(_tk, 7)
        r_dense_x = -0.000514642 + 1.00011 * jax.random.normal(jax.random.fold_in(_rk, 101), (512, 128), jnp.float32)
        W_top1 = 0.0456912 * jax.random.normal(jax.random.fold_in(_tk, 801), (479, 512), jnp.float32)
        W_top2 = 0.0441942 * jax.random.normal(jax.random.fold_in(_tk, 802), (512, 256), jnp.float32)
        W_top3 = 0.0625 * jax.random.normal(jax.random.fold_in(_tk, 803), (256, 1), jnp.float32)
        b_top1 = jnp.zeros((512,), jnp.float32)
        b_top2 = jnp.zeros((256,), jnp.float32)
        return (r_dense_x, ids, tbl_0, tbl_1, tbl_2, tbl_3, tbl_4, tbl_5, tbl_6, tbl_7, tbl_8, tbl_9, tbl_10, tbl_11, tbl_12, tbl_13, tbl_14, tbl_15, tbl_16, tbl_17, tbl_18, tbl_19, tbl_20, tbl_21, tbl_22, tbl_23, tbl_24, tbl_25, W_top1, b_top1, W_top2, b_top2, W_top3)
    r_dense_x, ids, tbl_0, tbl_1, tbl_2, tbl_3, tbl_4, tbl_5, tbl_6, tbl_7, tbl_8, tbl_9, tbl_10, tbl_11, tbl_12, tbl_13, tbl_14, tbl_15, tbl_16, tbl_17, tbl_18, tbl_19, tbl_20, tbl_21, tbl_22, tbl_23, tbl_24, tbl_25, W_top1, b_top1, W_top2, b_top2, W_top3 = _rec_inputs()

    def _L0_rec_setup():
        import jax, jax.numpy as jnp
        import numpy as np
        F = 26
        D = 128
        B = 2048
        _TRIU_I, _TRIU_J = np.triu_indices(F + 1, k=1)
        _TRIU_I = jnp.asarray(_TRIU_I)
        _TRIU_J = jnp.asarray(_TRIU_J)
        key = jax.random.key(seed)
        k1, k2 = jax.random.split(key)
        sparse_x = jax.random.normal(k1, (B, F, D), dtype=jnp.float32)
        dense_x = jax.random.normal(k2, (B, D), dtype=jnp.float32)
        return {'sparse_x': sparse_x, 'dense_x': dense_x}
    _L0_rec_all = _L0_rec_setup()
    _L0_rec_in = {k: v for k, v in _L0_rec_all.items() if k in ()}
    del _L0_rec_all
    return {'r_dense_x': r_dense_x, 'ids': ids, 'tbl_0': tbl_0, 'tbl_1': tbl_1, 'tbl_2': tbl_2, 'tbl_3': tbl_3, 'tbl_4': tbl_4, 'tbl_5': tbl_5, 'tbl_6': tbl_6, 'tbl_7': tbl_7, 'tbl_8': tbl_8, 'tbl_9': tbl_9, 'tbl_10': tbl_10, 'tbl_11': tbl_11, 'tbl_12': tbl_12, 'tbl_13': tbl_13, 'tbl_14': tbl_14, 'tbl_15': tbl_15, 'tbl_16': tbl_16, 'tbl_17': tbl_17, 'tbl_18': tbl_18, 'tbl_19': tbl_19, 'tbl_20': tbl_20, 'tbl_21': tbl_21, 'tbl_22': tbl_22, 'tbl_23': tbl_23, 'tbl_24': tbl_24, 'tbl_25': tbl_25, 'W_top1': W_top1, 'b_top1': b_top1, 'W_top2': W_top2, 'b_top2': b_top2, 'W_top3': W_top3}

def reference(r_dense_x, ids, tbl_0, tbl_1, tbl_2, tbl_3, tbl_4, tbl_5, tbl_6, tbl_7, tbl_8, tbl_9, tbl_10, tbl_11, tbl_12, tbl_13, tbl_14, tbl_15, tbl_16, tbl_17, tbl_18, tbl_19, tbl_20, tbl_21, tbl_22, tbl_23, tbl_24, tbl_25, W_top1, b_top1, W_top2, b_top2, W_top3):
    import jax
    import jax.numpy as jnp

    def _L0_rec_ref(sparse_x, dense_x):
        import jax, jax.numpy as jnp
        import numpy as np
        F = 26
        D = 128
        B = 2048
        _TRIU_I, _TRIU_J = np.triu_indices(F + 1, k=1)
        _TRIU_I = jnp.asarray(_TRIU_I)
        _TRIU_J = jnp.asarray(_TRIU_J)
        combined = jnp.concatenate([sparse_x, dense_x[:, None, :]], axis=1)
        interact = jnp.einsum('bfd,bgd->bfg', combined, combined)
        return interact[:, _TRIU_I, _TRIU_J]
    e = jnp.stack([tbl_0[ids[:, 0]], tbl_1[ids[:, 1]], tbl_2[ids[:, 2]], tbl_3[ids[:, 3]], tbl_4[ids[:, 4]], tbl_5[ids[:, 5]], tbl_6[ids[:, 6]], tbl_7[ids[:, 7]], tbl_8[ids[:, 8]], tbl_9[ids[:, 9]], tbl_10[ids[:, 10]], tbl_11[ids[:, 11]], tbl_12[ids[:, 12]], tbl_13[ids[:, 13]], tbl_14[ids[:, 14]], tbl_15[ids[:, 15]], tbl_16[ids[:, 16]], tbl_17[ids[:, 17]], tbl_18[ids[:, 18]], tbl_19[ids[:, 19]], tbl_20[ids[:, 20]], tbl_21[ids[:, 21]], tbl_22[ids[:, 22]], tbl_23[ids[:, 23]], tbl_24[ids[:, 24]], tbl_25[ids[:, 25]]], axis=1)
    z = _L0_rec_ref(e, r_dense_x)
    z = z.reshape(z.shape[0], -1)
    h = jnp.concatenate([z, r_dense_x], axis=1)
    h = jnp.maximum(h @ W_top1 + b_top1, 0.0)
    h = jnp.maximum(h @ W_top2 + b_top2, 0.0)
    y = h @ W_top3
    return y

_drawn_inputs = setup_inputs


def setup_inputs(seed=0):
    import zlib

    import numpy as np

    out = dict(_drawn_inputs(seed))
    spreads = {'b_top1': (0.0, 0.1), 'b_top2': (0.0, 0.1)}
    factors = {}
    for name, (base, spread) in spreads.items():
        noise = np.random.default_rng([zlib.crc32(name.encode()), seed]).standard_normal(out[name].shape)
        drawn = base * np.exp(spread * noise) if base else spread * noise
        out[name] = jnp.asarray(drawn.astype(out[name].dtype))
    for name, factor in factors.items():
        out[name] = (out[name] * factor).astype(out[name].dtype)
    return out
```

```python
import numpy as np
from contextlib import ExitStack
import concourse.bass as bass
from concourse import mybir

F32 = mybir.dt.float32
BF16 = mybir.dt.bfloat16
I32 = mybir.dt.int32
I16 = mybir.dt.int16
ALU = mybir.AluOpType
ACT = mybir.ActivationFunctionType

P = 128
B = 512
D = 128
FEATURES = 26
ROWS = [1250, 1250, 1250, 12500, 125000, 1000, 1000, 1000, 1250, 12500, 1250, 1250, 1000,
        1250, 1000, 1250, 1000, 1250, 1250, 12500, 1250, 1000, 1250, 1250, 1250, 1250]
ONEHOT = [5, 6, 7, 12, 14]
GATHERED = [f for f in range(FEATURES) if f not in ONEHOT]
NG, NH = len(GATHERED), len(ONEHOT)
SLOTS = NG + NH + 1
SLOT_FEATURE = GATHERED + ONEHOT + [FEATURES]
PAD = 32

VH = 1000
HC = 8
HP = VH // HC
PARTS = 3

SG = P // NG
NGATHER = -(-B // SG)
STEP_SAMPLES = 2 * SG
STEPS = -(-B // STEP_SAMPLES)
GROUP = 4
UNITS = -(-STEPS // 2)

CQ = 7
XROWS = PAD - SLOTS
H1, H2 = 512, 256
C1, C2 = H1 // P, H2 // P
BLOCK_STEPS = 10
BLOCKS = -(-STEPS // BLOCK_STEPS)
BN = BLOCK_STEPS * STEP_SAMPLES

G_RING = 20
G_SEMS = 8


def gather_samples(g):
    return min(SG, B - g * SG)


def step_samples(k):
    return min(STEP_SAMPLES, B - k * STEP_SAMPLES)


def step_gathers(k):
    return [g for g in (2 * k, 2 * k + 1) if g < NGATHER]


def block_samples(n):
    return min(BN, B - n * BN)


def block_units(n):
    return min((n + 1) * BLOCK_STEPS // 2, UNITS)


def columns(j):
    return min(CQ, SLOTS - j * CQ)


def tower(nc, table, gather_ids, gather_rows, hot_tables, hot_ids, x_t, x_rows, w1, b1, w2, b2, w3, out):
    with ExitStack() as ctx:
        def sb(name, shape, dt):
            return ctx.enter_context(nc.sbuf_tensor(name, shape, dt))

        def pb(name, shape, dt):
            return ctx.enter_context(nc.psum_tensor(name, shape, dt))

        def sem(name):
            return ctx.enter_context(nc.semaphore(name))

        ids_raw = sb("ids_raw", [SG * NG, NGATHER], I32)
        ids_rows = sb("ids_rows", [SG * NG, 2], F32)
        ids_clamped = sb("ids_clamped", [SG * NG, NGATHER], I32)
        row_ids = sb("row_ids", [SG * NG, NGATHER], I32)
        gathered = sb("gathered", [SG * NG, G_RING * 2, D], F32)
        identity = sb("identity", [P, P], F32)

        hot_raw = sb("hot_raw", [HP, NH, B], I32)
        hot_clamped = sb("hot_clamped", [HP, NH, B], I16)
        chunk_row_i = sb("chunk_row_i", [HP, HC], I32)
        chunk_row = sb("chunk_row", [HP, HC], F32)
        tab = sb("tab", [HP, NH, HC * D], F32)
        part = sb("part", [HP, 2, PARTS, HC * D], BF16)
        mask = sb("mask", [HP, 2, HC, B], BF16)

        x_sb = sb("x_sb", [D, B], F32)
        emb = sb("emb", [D, B, PAD], F32)
        z = sb("z", [P, CQ, B], F32)
        w1_sb = sb("w1_sb", [P, CQ, H1], F32)
        w2_sb = sb("w2_sb", [P, C1, H2], F32)
        w3_sb = sb("w3_sb", [P, C2], F32)
        b1_sb = sb("b1_sb", [P, C1], F32)
        b2_sb = sb("b2_sb", [P, C2], F32)
        h1 = sb("h1", [P, C1, BN], F32)
        h2 = sb("h2", [P, C2, BN], F32)
        y = sb("y", [1, B], F32)

        p_t = pb("p_t", [P, 2, 512], F32)
        p_z = pb("p_z", [P, 4, 512], F32)
        p_a = pb("p_a", [P, 512], F32)
        p_b = pb("p_b", [P, 512], F32)
        p_hot = [p_a, p_b]

        ids_in = sem("ids_in")
        hot_ids_in = sem("hot_ids_in")
        tab_in = [sem(f"tab_in{e}") for e in range(NH)]
        x_in = sem("x_in")
        dense_in = sem("dense_in")
        iota_done = sem("iota_done")
        zeroed = sem("zeroed")
        identity_ready = sem("identity_ready")
        ids_step = sem("ids_step")
        ids_ready = sem("ids_ready")
        gather_in = [sem(f"gather_in{i}") for i in range(G_SEMS)]
        chunk_row_ready = sem("chunk_row_ready")
        hot_ids_ready = sem("hot_ids_ready")
        mask_ready = sem("mask_ready")
        high_ready = sem("high_ready")
        rest_ready = sem("rest_ready")
        mid_ready = sem("mid_ready")
        low_ready = sem("low_ready")
        hot_done = sem("hot_done")
        hot_copied = sem("hot_copied")
        pad_ready = sem("pad_ready")
        x_copied = sem("x_copied")
        t_done = sem("t_done")
        t_copied = sem("t_copied")
        inter_done = sem("inter_done")
        z_low_copied = sem("z_low_copied")
        z_high_copied = sem("z_high_copied")
        z_pad_ready = sem("z_pad_ready")
        l1_done = sem("l1_done")
        h1_ready = sem("h1_ready")
        l2_done = sem("l2_done")
        h2_ready = sem("h2_ready")
        l3_done = sem("l3_done")
        y_ready = sem("y_ready")
        out_done = sem("out_done")
        N_DENSE = 9

        def copy_interactions(copy, u, quadrants, signal):
            steps = [k for k in (2 * u, 2 * u + 1) if k < STEPS]
            groups = step_samples(steps[0]) // GROUP
            bank = 2 * (u % 2)
            for s in quadrants:
                src = p_z[32 * s:32 * s + SLOTS, bank:bank + len(steps), 0:groups * GROUP * SLOTS]
                src = src.rearrange("p k (g c) -> p k g c", g=groups)
                first = 2 * u * STEP_SAMPLES
                for j in range(4):
                    dst = z[32 * j:32 * j + SLOTS, 0:columns(j), first:first + len(steps) * groups * GROUP]
                    dst = dst.rearrange("p t (k g s) -> p k g t s", k=len(steps), s=GROUP)
                    c = s * SLOTS + j * CQ
                    for i in range(len(steps)):
                        last = copy(dst[:, i, :, :, s], src[:, i, :, c:c + columns(j)])
            last.then_inc(signal, 1)

        block = ctx.enter_context(nc.Block())

        @block.sync
        def _(sp):
            sp.dma_start(ids_raw[:], gather_ids).then_inc(ids_in, 16)
            sp.dma_start(ids_rows[:], gather_rows).then_inc(ids_in, 16)
            sp.dma_start(tab[:, 0, :], hot_tables[0]).then_inc(tab_in[0], 16)
            for e in range(1, NH):
                sp.dma_start(tab[:, e, :], hot_tables[e]).then_inc(tab_in[e], 16)
            for j in range(4):
                n = columns(j)
                sp.dma_start(z[32 * j + SLOTS:32 * j + PAD, 0:n, :], x_rows[j, :, 0:n, :]).then_inc(dense_in, 16)
            sp.dma_start(w1_sb[:], w1).then_inc(dense_in, 16)
            sp.dma_start(w2_sb[:], w2).then_inc(dense_in, 16)
            sp.dma_start(w3_sb[:], w3).then_inc(dense_in, 16)
            sp.dma_start(b1_sb[:], b1).then_inc(dense_in, 16)
            sp.dma_start(b2_sb[:], b2).then_inc(dense_in, 16)
            sp.wait_ge(y_ready, BLOCKS)
            sp.dma_start(out, y[:]).then_inc(out_done, 16)
            sp.wait_ge(out_done, 16)

        @block.gpsimd
        def _(pool):
            nc.gpsimd.iota(chunk_row_i[:], [[1, HC]], base=0, channel_multiplier=HC).then_inc(iota_done, 1)
            nc.gpsimd.memset(identity[:], 0.0).then_inc(zeroed, 1)
            pool.wait_ge(zeroed, 1)
            nc.gpsimd.affine_select(out=identity[:], in_=identity[:], compare_op=ALU.not_equal, fill=1.0,
                                    base=0, pattern=[[-1, P]], channel_multiplier=1).then_inc(identity_ready, 1)
            pool.wait_ge(ids_ready, 1)
            for k in range(STEPS):
                if k >= G_SEMS:
                    pool.wait_ge(gather_in[k % G_SEMS], 32 * (k // G_SEMS))
                if k >= G_RING:
                    pool.wait_ge(t_done, k - G_RING + 1)
                for g in step_gathers(k):
                    rows = gather_samples(g) * NG
                    nc.gpsimd.indirect_dma_start(
                        gathered[0:rows, g % (2 * G_RING), :], None, table,
                        bass.IndirectOffsetOnAxis(row_ids[0:rows, g:g + 1], 0)).then_inc(gather_in[k % G_SEMS], 16)

        @block.vector
        def _(dve):
            dve.wait_ge(ids_in, 32)
            nc.vector.tensor_scalar(ids_clamped[:], ids_raw[:], 0.0, ids_rows[:, 0:1], ALU.max, ALU.min).then_inc(ids_step, 1)
            dve.wait_ge(ids_step, 1)
            nc.vector.tensor_scalar(row_ids[:], ids_clamped[:], ids_rows[:, 1:2], None, ALU.add).then_inc(ids_ready, 1)
            dve.wait_ge(iota_done, 1)
            nc.vector.tensor_copy(chunk_row[:], chunk_row_i[:]).then_inc(chunk_row_ready, 1)
            dve.wait_ge(chunk_row_ready, 1)
            for e in range(NH):
                if e == 0:
                    dve.wait_ge(hot_ids_in, 16)
                nc.vector.tensor_scalar(hot_clamped[:, e, :], hot_raw[:, e, :], 0, VH - 1, ALU.max, ALU.min).then_inc(hot_ids_ready, 1)
                dve.wait_ge(hot_ids_ready, e + 1)
                if e >= 2:
                    dve.wait_ge(hot_done, e - 1)
                for c in range(HC):
                    last = nc.vector.tensor_scalar(mask[:, e % 2, c, :], hot_clamped[:, e, :], chunk_row[:, c:c + 1],
                                                   None, ALU.is_equal)
                last.then_inc(mask_ready, 1)
                dve.wait_ge(high_ready, e + 1)
                nc.vector.tensor_tensor(tab[:, e, :], tab[:, e, :], part[:, e % 2, 0, :], ALU.subtract).then_inc(rest_ready, 1)
                dve.wait_ge(mid_ready, e + 1)
                nc.vector.tensor_tensor(part[:, e % 2, 2, :], tab[:, e, :], part[:, e % 2, 1, :], ALU.subtract).then_inc(low_ready, 1)
                if e == 0:
                    nc.vector.memset(z[96:128, CQ - 1, :], 0.0).then_inc(z_pad_ready, 1)
                    nc.vector.memset(emb[:, :, SLOTS:PAD], 0.0).then_inc(pad_ready, 1)

            def layer1_out(n):
                dve.wait_ge(l1_done, n + 1)
                if n >= 1:
                    dve.wait_ge(l2_done, n)
                size = block_samples(n)
                for c in range(C1):
                    last = nc.vector.tensor_scalar(h1[0:64, c, 0:size], p_a[0:64, c * BN:c * BN + size],
                                                   b1_sb[0:64, c:c + 1], 0.0, ALU.add, ALU.max)
                last.then_inc(h1_ready, 1)

            dve.wait_ge(dense_in, 16 * N_DENSE)
            n = 0
            for u in range(UNITS):
                dve.wait_ge(inter_done, u + 1)
                copy_interactions(nc.vector.tensor_copy, u, (0, 1), z_low_copied)
                if n < BLOCKS - 1 and u == block_units(n) + 1:
                    layer1_out(n)
                    n += 1
            layer1_out(BLOCKS - 1)

        @block.scalar
        def _(act):
            act.dma_start(hot_raw[:], hot_ids).then_inc(hot_ids_in, 16)
            act.dma_start(x_sb[:], x_t).then_inc(x_in, 16)

            def cut(e):
                act.wait_ge(tab_in[e], 16)
                if e >= 2:
                    act.wait_ge(hot_done, e - 1)
                nc.scalar.copy(part[:, e % 2, 0, :], tab[:, e, :]).then_inc(high_ready, 1)
                act.wait_ge(rest_ready, e + 1)
                nc.scalar.copy(part[:, e % 2, 1, :], tab[:, e, :]).then_inc(mid_ready, 1)

            def copy_hot(e):
                act.wait_ge(hot_done, e + 1)
                nc.scalar.copy(emb[:, :, NG + e], p_hot[e % 2][:]).then_inc(hot_copied, 1)

            def copy_t(k):
                act.wait_ge(t_done, k + 1)
                n = step_samples(k)
                first = k * STEP_SAMPLES
                nc.scalar.copy(emb[:, first:first + n, 0:NG],
                               p_t[:, k % 2, 0:n * NG].rearrange("p (n f) -> p n f", f=NG)).then_inc(t_copied, 1)

            def layer1_out(n):
                act.wait_ge(l1_done, n + 1)
                if n >= 1:
                    act.wait_ge(l2_done, n)
                size = block_samples(n)
                for c in range(C1):
                    last = nc.scalar.activation(h1[64:128, c, 0:size], p_a[64:128, c * BN:c * BN + size],
                                                ACT.Relu, bias=b1_sb[64:128, c:c + 1])
                last.then_inc(h1_ready, 1)

            def layer2_out(n):
                act.wait_ge(l2_done, n + 1)
                if n >= 1:
                    act.wait_ge(l3_done, n)
                size = block_samples(n)
                for c in range(C2):
                    last = nc.scalar.activation(h2[:, c, 0:size], p_b[:, c * BN:c * BN + size],
                                                ACT.Relu, bias=b2_sb[:, c:c + 1])
                last.then_inc(h2_ready, 1)

            def layer3_out(n):
                act.wait_ge(l3_done, n + 1)
                size = block_samples(n)
                nc.scalar.copy(y[:, n * BN:n * BN + size], p_b[0:1, C2 * BN:C2 * BN + size]).then_inc(y_ready, 1)

            cut(0)
            cut(1)
            act.wait_ge(x_in, 16)
            nc.scalar.copy(emb[:, :, SLOTS - 1], x_sb[:]).then_inc(x_copied, 1)
            for what, i in ORDER:
                if what == "hot":
                    copy_hot(i)
                    if i + 2 < NH:
                        cut(i + 2)
                if what == "transpose":
                    copy_t(i)
                if what == "interact" and (i % 2 == 1 or i == STEPS - 1):
                    if i == 1:
                        act.wait_ge(dense_in, 16 * N_DENSE)
                    u = i // 2
                    act.wait_ge(inter_done, u + 1)
                    copy_interactions(nc.scalar.copy, u, (2, 3), z_high_copied)
                if what == "layer1":
                    layer1_out(i)
                if what == "layer2":
                    layer2_out(i)
                if what == "layer3":
                    layer3_out(i)

        @block.tensor
        def _(pe):
            def one_hot(e):
                if e >= 2:
                    pe.wait_ge(hot_copied, e - 1)
                pe.wait_ge(mask_ready, e + 1)
                for i, ready in enumerate((high_ready, mid_ready, low_ready)):
                    pe.wait_ge(ready, e + 1)
                    for c in range(HC):
                        last = nc.tensor.matmul(p_hot[e % 2][:], part[:, e % 2, i, c * D:(c + 1) * D], mask[:, e % 2, c, :],
                                                start=(i == 0 and c == 0), stop=(i == PARTS - 1 and c == HC - 1))
                last.then_inc(hot_done, 1)

            def transpose(k):
                if k == 0:
                    pe.wait_ge(identity_ready, 1)
                pe.wait_ge(gather_in[k % G_SEMS], 16 * len(step_gathers(k)) + 32 * (k // G_SEMS))
                if k >= 2:
                    pe.wait_ge(t_copied, k - 1)
                at = 0
                for g in step_gathers(k):
                    rows = gather_samples(g) * NG
                    last = nc.tensor.transpose(p_t[:, k % 2, at:at + rows], gathered[0:rows, g % (2 * G_RING), :],
                                               identity[0:rows, 0:rows])
                    at += rows
                last.then_inc(t_done, 1)

            def interact(k):
                if k == 0:
                    pe.wait_ge(hot_copied, NH)
                    pe.wait_ge(pad_ready, 1)
                    pe.wait_ge(x_copied, 1)
                if k % 2 == 0 and k >= 4:
                    pe.wait_ge(z_low_copied, k // 2 - 1)
                    pe.wait_ge(z_high_copied, k // 2 - 1)
                pe.wait_ge(t_copied, k + 1)
                for g in range(step_samples(k) // GROUP):
                    first = k * STEP_SAMPLES + g * GROUP
                    w = GROUP * SLOTS
                    last = nc.tensor.matmul(p_z[:, k % 4, g * w:(g + 1) * w], emb[:, first:first + GROUP, :],
                                            emb[:, first:first + GROUP, 0:SLOTS], start=True, stop=True)
                if k % 2 == 1 or k == STEPS - 1:
                    last.then_inc(inter_done, 1)

            def layer1(n):
                pe.wait_ge(z_low_copied, block_units(n))
                pe.wait_ge(z_high_copied, block_units(n))
                if n == 0:
                    pe.wait_ge(dense_in, 16 * N_DENSE)
                    pe.wait_ge(z_pad_ready, 1)
                else:
                    pe.wait_ge(h1_ready, 2 * n)
                size = block_samples(n)
                for c in range(C1):
                    for t in range(CQ):
                        last = nc.tensor.matmul(p_a[:, c * BN:c * BN + size], w1_sb[:, t, c * P:(c + 1) * P],
                                                z[:, t, n * BN:n * BN + size], start=(t == 0), stop=(t == CQ - 1))
                last.then_inc(l1_done, 1)

            def layer2(n):
                pe.wait_ge(h1_ready, 2 * (n + 1))
                if n >= 1:
                    pe.wait_ge(y_ready, n)
                size = block_samples(n)
                for m in range(C2):
                    for c in range(C1):
                        last = nc.tensor.matmul(p_b[:, m * BN:m * BN + size], w2_sb[:, c, m * P:(m + 1) * P],
                                                h1[:, c, 0:size], start=(c == 0), stop=(c == C1 - 1))
                last.then_inc(l2_done, 1)

            def layer3(n):
                pe.wait_ge(h2_ready, n + 1)
                size = block_samples(n)
                for c in range(C2):
                    last = nc.tensor.matmul(p_b[0:1, C2 * BN:C2 * BN + size], w3_sb[:, c:c + 1], h2[:, c, 0:size],
                                            start=(c == 0), stop=(c == C2 - 1))
                last.then_inc(l3_done, 1)

            for what, i in ORDER:
                if what == "hot":
                    one_hot(i)
                if what == "transpose":
                    transpose(i)
                if what == "interact":
                    interact(i)
                if what == "layer1":
                    layer1(i)
                if what == "layer2":
                    layer2(i)
                if what == "layer3":
                    layer3(i)


def order():
    todo = []
    ahead = [1, 3, 6, 8, 11]
    t = 0
    for e in range(NH):
        todo.append(("hot", e))
        while t < ahead[e]:
            todo.append(("transpose", t))
            t += 1
    n1 = n2 = n3 = 0
    for k in range(STEPS):
        while t < min(k + 2, STEPS):
            todo.append(("transpose", t))
            t += 1
        todo.append(("interact", k))
        if n3 < n2:
            todo.append(("layer3", n3))
            n3 += 1
        elif n2 < n1:
            todo.append(("layer2", n2))
            n2 += 1
        elif n1 < BLOCKS - 1 and k >= 2 * block_units(n1) + 2:
            todo.append(("layer1", n1))
            n1 += 1
    while n3 < BLOCKS:
        if n3 < n2:
            todo.append(("layer3", n3))
            n3 += 1
        elif n2 < n1:
            todo.append(("layer2", n2))
            n2 += 1
        else:
            todo.append(("layer1", n1))
            n1 += 1
    return todo


ORDER = order()


def kernel(**inputs):
    import concourse.bacc as bacc
    from concourse.bass_utils import run_bass_kernel_spmd as run

    a = {name: np.asarray(v) for name, v in inputs.items()}
    ids = a["ids"]

    table = np.concatenate([a[f"tbl_{f}"] for f in GATHERED])
    padded = np.zeros((NGATHER * SG, NG), ids.dtype)
    padded[:B] = ids[:, GATHERED]
    gather_ids = padded.reshape(NGATHER, SG * NG).T
    rows = [ROWS[f] for f in GATHERED]
    first = [sum(rows[:i]) for i in range(NG)]
    gather_rows = np.array([[r - 1, s] for r, s in zip(rows, first)] * SG, np.float32)

    hot_tables = np.stack([a[f"tbl_{f}"].reshape(HP, HC * D) for f in ONEHOT])
    hot_ids = ids[:, ONEHOT].T

    x = a["r_dense_x"]
    w1 = np.zeros((4, PAD, CQ, H1), np.float32)
    x_rows = np.zeros((4, XROWS, CQ, B), np.float32)
    pair = {}
    for i in range(FEATURES + 1):
        for j in range(i + 1, FEATURES + 1):
            pair[i, j] = len(pair)
    for q in range(1, SLOTS):
        for p in range(q):
            w1[q // CQ, p, q % CQ] = a["W_top1"][pair[tuple(sorted((SLOT_FEATURE[p], SLOT_FEATURE[q])))]]
    for d in range(D):
        c, r = divmod(d, XROWS)
        w1[c // CQ, SLOTS + r, c % CQ] = a["W_top1"][len(pair) + d]
        x_rows[c // CQ, r, c % CQ] = x[:, d]

    arrays = {
        "table": table,
        "gather_ids": gather_ids,
        "gather_rows": gather_rows,
        "hot_tables": hot_tables,
        "hot_ids": hot_ids.reshape(1, NH * B),
        "x_t": x.T,
        "x_rows": x_rows,
        "w1": w1.reshape(P, CQ, H1),
        "b1": a["b_top1"].reshape(C1, P).T,
        "w2": a["W_top2"].reshape(C1, P, H2).transpose(1, 0, 2),
        "b2": a["b_top2"].reshape(C2, P).T,
        "w3": a["W_top3"].reshape(C2, P).T,
    }
    arrays = {f"in_{name}": np.ascontiguousarray(v) for name, v in arrays.items()}
    nc = bacc.Bacc("TRN2", target_bir_lowering=False, num_devices=1)
    args = {name[3:]: nc.dram_tensor(name, v.shape, mybir.dt.from_np(v.dtype), kind="ExternalInput").ap()
            for name, v in arrays.items()}
    args["hot_ids"] = args["hot_ids"].rearrange("o (e b) -> (o e) b", e=NH).partition_broadcast(HP)
    out = nc.dram_tensor("out_y", (1, B), F32, kind="ExternalOutput").ap()
    tower(nc, out=out, **args)
    result = run(nc, [arrays], core_ids=[0]).results[0]["out_y"]
    return result.reshape(B, 1)
```

```python
import numpy as np
from contextlib import ExitStack
import concourse.bass as bass
from concourse import mybir

F32 = mybir.dt.float32
BF16 = mybir.dt.bfloat16
I32 = mybir.dt.int32
I16 = mybir.dt.int16
ALU = mybir.AluOpType
ACT = mybir.ActivationFunctionType

P = 128
B = 512
D = 128
FEATURES = 26
ROWS = [1250, 1250, 1250, 12500, 125000, 1000, 1000, 1000, 1250, 12500, 1250, 1250, 1000,
        1250, 1000, 1250, 1000, 1250, 1250, 12500, 1250, 1000, 1250, 1250, 1250, 1250]
ONEHOT = [5, 6, 7, 12, 14]
GATHERED = [f for f in range(FEATURES) if f not in ONEHOT]
NG, NH = len(GATHERED), len(ONEHOT)
SLOTS = NG + NH + 1
SLOT_FEATURE = GATHERED + ONEHOT + [FEATURES]
PAD = 32

VH = 1000
HC = 8
HP = VH // HC
PARTS = 3

SG = P // NG
NGATHER = -(-B // SG)
STEP_SAMPLES = 2 * SG
STEPS = -(-B // STEP_SAMPLES)
GROUP = 4
PAIR = 2
UNITS = -(-STEPS // 2)

CQ = 7
XROWS = PAD - SLOTS
H1, H2 = 512, 256
C1, C2 = H1 // P, H2 // P
BN = 128
BLOCKS = B // BN

G_RING = 12
G_SEMS = 8
T_RING = 2
Z_RING = 3
WARM = 12
H_RING = 2


def gather_samples(g):
    return min(SG, B - g * SG)


def step_samples(k):
    return min(STEP_SAMPLES, B - k * STEP_SAMPLES)


def step_gathers(k):
    return [g for g in (2 * k, 2 * k + 1) if g < NGATHER]


def block_units(n):
    return -(-(n + 1) * BN // (2 * STEP_SAMPLES))


def columns(j):
    return min(CQ, SLOTS - j * CQ)


def tower(nc, table, gather_ids, gather_rows, hot_tables, hot_ids, x_t, x_rows, w1, b1, w2, b2, w3, out):
    with ExitStack() as ctx:
        def sb(name, shape, dt):
            return ctx.enter_context(nc.sbuf_tensor(name, shape, dt))

        def pb(name, shape, dt):
            return ctx.enter_context(nc.psum_tensor(name, shape, dt))

        def sem(name):
            return ctx.enter_context(nc.semaphore(name))

        ids_raw = sb("ids_raw", [SG * NG, NGATHER], I32)
        ids_rows = sb("ids_rows", [SG * NG, 2], F32)
        ids_clamped = sb("ids_clamped", [SG * NG, NGATHER], I32)
        row_ids = sb("row_ids", [SG * NG, NGATHER], I32)
        gathered = sb("gathered", [SG * NG, G_RING * 2, D], F32)
        identity = sb("identity", [P, P], F32)
        blank = sb("blank", [P, 512], BF16)

        hot_raw = sb("hot_raw", [HP, NH, B], I32)
        hot_clamped = sb("hot_clamped", [HP, NH, B], I16)
        chunk_row_i = sb("chunk_row_i", [HP, HC], I32)
        chunk_row = sb("chunk_row", [HP, HC], F32)
        tab = sb("tab", [HP, NH, HC * D], F32)
        part = sb("part", [HP, NH, PARTS, HC * D], BF16)
        mask = sb("mask", [HP, H_RING, HC, B], BF16)

        x_sb = sb("x_sb", [D, B], F32)
        emb = sb("emb", [D, B, PAD], F32)
        z = sb("z", [P, CQ, B], F32)
        w1_sb = sb("w1_sb", [P, CQ, H1], F32)
        w2_sb = sb("w2_sb", [P, C1, H2], F32)
        w3_sb = sb("w3_sb", [P, C2], F32)
        b1_sb = sb("b1_sb", [P, C1], F32)
        b2_sb = sb("b2_sb", [P, C2], F32)
        h1 = sb("h1", [P, C1, BN], F32)
        h2 = sb("h2", [P, C2, BN], F32)
        y = sb("y", [1, B], F32)

        p_t = pb("p_t", [P, T_RING, 512], F32)
        p_z = pb("p_z", [P, Z_RING, 512], F32)
        p_1 = pb("p_1", [P, 2, 512], F32)
        p_2 = pb("p_2", [P, 512], F32)

        ids_in = sem("ids_in")
        hot_ids_in = [sem(f"hot_ids_in{e}") for e in range(NH)]
        tab_in = [sem(f"tab_in{e}") for e in range(NH)]
        tab_half_in = sem("tab_half_in")
        x_in = sem("x_in")
        dense_in = sem("dense_in")
        blank_ready = sem("blank_ready")
        iota_done = sem("iota_done")
        zeroed = sem("zeroed")
        identity_ready = sem("identity_ready")
        ids_step = sem("ids_step")
        ids_ready = sem("ids_ready")
        gather_in = [sem(f"gather_in{i}") for i in range(G_SEMS)]
        chunk_row_ready = sem("chunk_row_ready")
        hot_ids_ready = sem("hot_ids_ready")
        mask_ready = sem("mask_ready")
        high_ready = sem("high_ready")
        rest_ready = sem("rest_ready")
        mid_ready = sem("mid_ready")
        low_ready = sem("low_ready")
        hot_done = sem("hot_done")
        hot_copied = sem("hot_copied")
        pad_ready = sem("pad_ready")
        x_copied = sem("x_copied")
        t_done = sem("t_done")
        t_copied = sem("t_copied")
        inter_done = sem("inter_done")
        z_low_copied = sem("z_low_copied")
        z_high_copied = sem("z_high_copied")
        z_pad_ready = sem("z_pad_ready")
        l1_done = sem("l1_done")
        h1_ready = sem("h1_ready")
        l2_done = sem("l2_done")
        h2_ready = sem("h2_ready")
        l3_done = sem("l3_done")
        y_ready = sem("y_ready")
        out_done = sem("out_done")
        N_DENSE = 9

        def copy_interactions(copy, u, quadrants, signal):
            steps = [k for k in (2 * u, 2 * u + 1) if k < STEPS]
            count = sum(step_samples(k) for k in steps) // GROUP
            first = 2 * u * STEP_SAMPLES
            for s in quadrants:
                src = p_z[32 * s:32 * s + SLOTS, u % Z_RING, 0:count * PAIR * SLOTS].rearrange("p (g c) -> p g c", g=count)
                for j in range(4):
                    dst = z[32 * j:32 * j + SLOTS, 0:columns(j), first:first + count * GROUP]
                    dst = dst.rearrange("p t (g s) -> p g t s", s=GROUP)
                    c = (s % PAIR) * SLOTS + j * CQ
                    last = copy(dst[:, :, :, s], src[:, :, c:c + columns(j)])
            last.then_inc(signal, 1)

        def half(h):
            return slice(h * HC * D // 2, (h + 1) * HC * D // 2)

        block = ctx.enter_context(nc.Block())

        @block.sync
        def _(sp):
            sp.dma_start(ids_raw[:], gather_ids).then_inc(ids_in, 16)
            sp.dma_start(hot_raw[:, 0, :], hot_ids[:, 0, :]).then_inc(hot_ids_in[0], 16)
            sp.dma_start(tab[:, 0, half(1)], hot_tables[0][:, half(1)]).then_inc(tab_half_in, 16)
            for e in range(1, NH):
                sp.dma_start(hot_raw[:, e, :], hot_ids[:, e, :]).then_inc(hot_ids_in[e], 16)
                sp.dma_start(tab[:, e, :], hot_tables[e]).then_inc(tab_in[e], 16)
            sp.dma_start(x_sb[:], x_t).then_inc(x_in, 16)
            sp.wait_ge(t_done, 5)
            for j in range(4):
                n = columns(j)
                sp.dma_start(z[32 * j + SLOTS:32 * j + PAD, 0:n, :], x_rows[j, :, 0:n, :]).then_inc(dense_in, 16)
            sp.dma_start(w1_sb[:], w1).then_inc(dense_in, 16)
            sp.dma_start(w2_sb[:], w2).then_inc(dense_in, 16)
            sp.dma_start(w3_sb[:], w3).then_inc(dense_in, 16)
            sp.dma_start(b1_sb[:], b1).then_inc(dense_in, 16)
            sp.dma_start(b2_sb[:], b2).then_inc(dense_in, 16)
            sp.wait_ge(y_ready, BLOCKS)
            sp.dma_start(out, y[:]).then_inc(out_done, 16)
            sp.wait_ge(out_done, 16)

        @block.gpsimd
        def _(pool):
            nc.gpsimd.iota(chunk_row_i[:], [[1, HC]], base=0, channel_multiplier=HC).then_inc(iota_done, 1)
            nc.gpsimd.memset(identity[:], 0.0).then_inc(zeroed, 1)
            pool.wait_ge(zeroed, 1)
            nc.gpsimd.affine_select(out=identity[:], in_=identity[:], compare_op=ALU.not_equal, fill=1.0,
                                    base=0, pattern=[[-1, P]], channel_multiplier=1).then_inc(identity_ready, 1)
            pool.wait_ge(ids_ready, 1)
            for k in range(STEPS):
                if k >= G_SEMS:
                    pool.wait_ge(gather_in[k % G_SEMS], 32 * (k // G_SEMS))
                if k >= G_RING:
                    pool.wait_ge(t_done, k - G_RING + 1)
                for g in step_gathers(k):
                    rows = gather_samples(g) * NG
                    nc.gpsimd.indirect_dma_start(
                        gathered[0:rows, g % (2 * G_RING), :], None, table,
                        bass.IndirectOffsetOnAxis(row_ids[0:rows, g:g + 1], 0)).then_inc(gather_in[k % G_SEMS], 16)

        @block.vector
        def _(dve):
            nc.vector.memset(blank[:], 0.0).then_inc(blank_ready, 1)
            dve.wait_ge(ids_in, 32)
            nc.vector.tensor_scalar(ids_clamped[:], ids_raw[:], 0.0, ids_rows[:, 0:1], ALU.max, ALU.min).then_inc(ids_step, 1)
            dve.wait_ge(ids_step, 1)
            nc.vector.tensor_scalar(row_ids[:], ids_clamped[:], ids_rows[:, 1:2], None, ALU.add).then_inc(ids_ready, 1)
            dve.wait_ge(iota_done, 1)
            nc.vector.tensor_copy(chunk_row[:], chunk_row_i[:]).then_inc(chunk_row_ready, 1)
            dve.wait_ge(chunk_row_ready, 1)

            def make_mask(e):
                dve.wait_ge(hot_ids_in[e], 16)
                nc.vector.tensor_scalar(hot_clamped[:, e, :], hot_raw[:, e, :], 0, VH - 1, ALU.max, ALU.min).then_inc(hot_ids_ready, 1)
                dve.wait_ge(hot_ids_ready, e + 1)
                if e >= H_RING:
                    dve.wait_ge(hot_done, e - H_RING + 1)
                for c in range(HC):
                    nc.vector.tensor_scalar(mask[:, e % H_RING, c, :], hot_clamped[:, e, :], chunk_row[:, c:c + 1],
                                            None, ALU.is_equal).then_inc(mask_ready, 1)

            def make_rest(e):
                for h in range(2):
                    dve.wait_ge(high_ready, 2 * e + h + 1)
                    nc.vector.tensor_tensor(tab[:, e, half(h)], tab[:, e, half(h)], part[:, e, 0, half(h)],
                                            ALU.subtract).then_inc(rest_ready, 1)

            def make_low(e):
                for h in range(2):
                    dve.wait_ge(mid_ready, 2 * e + h + 1)
                    nc.vector.tensor_tensor(part[:, e, 2, half(h)], tab[:, e, half(h)], part[:, e, 1, half(h)],
                                            ALU.subtract).then_inc(low_ready, 1)

            make_mask(0)
            make_rest(0)
            make_low(0)
            make_mask(1)
            for e in range(1, NH):
                make_rest(e)
                if e + 1 < NH:
                    make_mask(e + 1)
                make_low(e)
            nc.vector.memset(z[96:128, CQ - 1, :], 0.0).then_inc(z_pad_ready, 1)
            nc.vector.memset(emb[:, :, SLOTS:PAD], 0.0).then_inc(pad_ready, 1)

            def layer1_out(n, bank):
                if n >= 1:
                    dve.wait_ge(l2_done, n)
                dve.wait_ge(l1_done, 2 * n + bank + 1)
                for c in (2 * bank, 2 * bank + 1):
                    at = c % 2 * BN
                    last = nc.vector.tensor_scalar(h1[0:64, c, 0:BN], p_1[0:64, c // 2, at:at + BN],
                                                   b1_sb[0:64, c:c + 1], 0.0, ALU.add, ALU.max)
                last.then_inc(h1_ready, 1)

            dve.wait_ge(dense_in, 16 * N_DENSE)
            for what, i in ORDER:
                if what == "interact" and (i % 2 == 1 or i == STEPS - 1):
                    dve.wait_ge(inter_done, i // 2 + 1)
                    copy_interactions(nc.vector.tensor_copy, i // 2, (0, 1), z_low_copied)
                if what == "layer1" and i % 2 == 1:
                    layer1_out(i // C1, i % C1 // 2)

        @block.scalar
        def _(act):
            act.dma_start(ids_rows[:], gather_rows).then_inc(ids_in, 16)
            act.dma_start(tab[:, 0, half(0)], hot_tables[0][:, half(0)]).then_inc(tab_in[0], 16)

            def cut_high(e):
                act.wait_ge(tab_in[e], 16)
                for h in range(2):
                    if e == 0 and h == 1:
                        act.wait_ge(tab_half_in, 16)
                    nc.scalar.copy(part[:, e, 0, half(h)], tab[:, e, half(h)]).then_inc(high_ready, 1)

            def cut_mid(e):
                for h in range(2):
                    act.wait_ge(rest_ready, 2 * e + h + 1)
                    nc.scalar.copy(part[:, e, 1, half(h)], tab[:, e, half(h)]).then_inc(mid_ready, 1)

            def copy_hot(e):
                act.wait_ge(hot_done, e + 1)
                nc.scalar.copy(emb[:, :, NG + e], p_1[:, e % 2, :]).then_inc(hot_copied, 1)

            def copy_t(k):
                act.wait_ge(t_done, k + 1)
                n = step_samples(k)
                first = k * STEP_SAMPLES
                nc.scalar.copy(emb[:, first:first + n, 0:NG],
                               p_t[:, k % T_RING, 0:n * NG].rearrange("p (n f) -> p n f", f=NG)).then_inc(t_copied, 1)

            def layer1_out(n, bank):
                if n >= 1:
                    act.wait_ge(l2_done, n)
                act.wait_ge(l1_done, 2 * n + bank + 1)
                for c in (2 * bank, 2 * bank + 1):
                    at = c % 2 * BN
                    last = nc.scalar.activation(h1[64:128, c, 0:BN], p_1[64:128, c // 2, at:at + BN],
                                                ACT.Relu, bias=b1_sb[64:128, c:c + 1])
                last.then_inc(h1_ready, 1)

            def layer2_out(n):
                act.wait_ge(l2_done, n + 1)
                if n >= 1:
                    act.wait_ge(l3_done, n)
                for c in range(C2):
                    last = nc.scalar.activation(h2[:, c, 0:BN], p_2[:, c * BN:(c + 1) * BN],
                                                ACT.Relu, bias=b2_sb[:, c:c + 1])
                last.then_inc(h2_ready, 1)

            def layer3_out(n):
                act.wait_ge(l3_done, n + 1)
                nc.scalar.copy(y[:, n * BN:(n + 1) * BN], p_2[0:1, 0:BN]).then_inc(y_ready, 1)

            cut_high(0)
            cut_mid(0)
            cut_high(1)
            act.wait_ge(x_in, 16)
            nc.scalar.copy(emb[:, :, SLOTS - 1], x_sb[:]).then_inc(x_copied, 1)
            for what, i in transposes_first(ORDER):
                if what == "hot":
                    if i + 2 < NH:
                        cut_high(i + 2)
                    if i + 1 < NH:
                        cut_mid(i + 1)
                    copy_hot(i)
                if what == "transpose":
                    copy_t(i)
                if what == "interact" and (i % 2 == 1 or i == STEPS - 1):
                    if i == 1:
                        act.wait_ge(dense_in, 16 * N_DENSE)
                    u = i // 2
                    act.wait_ge(inter_done, u + 1)
                    copy_interactions(nc.scalar.copy, u, (2, 3), z_high_copied)
                if what == "layer1" and i % 2 == 1:
                    layer1_out(i // C1, i % C1 // 2)
                if what == "layer2":
                    layer2_out(i)
                if what == "layer3":
                    layer3_out(i)

        @block.tensor
        def _(pe):
            def one_hot(e):
                if e >= 2:
                    pe.wait_ge(hot_copied, e - 1)
                for i, ready in enumerate((high_ready, mid_ready, low_ready)):
                    for c in range(HC):
                        if c % (HC // 2) == 0:
                            pe.wait_ge(ready, 2 * e + c // (HC // 2) + 1)
                        if i == 0:
                            pe.wait_ge(mask_ready, e * HC + c + 1)
                        last = nc.tensor.matmul(p_1[:, e % 2, :], part[:, e, i, c * D:(c + 1) * D], mask[:, e % H_RING, c, :],
                                                start=(i == 0 and c == 0), stop=(i == PARTS - 1 and c == HC - 1))
                last.then_inc(hot_done, 1)

            def transpose(k):
                if k == 0:
                    pe.wait_ge(identity_ready, 1)
                pe.wait_ge(gather_in[k % G_SEMS], 16 * len(step_gathers(k)) + 32 * (k // G_SEMS))
                if k >= T_RING:
                    pe.wait_ge(t_copied, k - T_RING + 1)
                at = 0
                for g in step_gathers(k):
                    rows = gather_samples(g) * NG
                    last = nc.tensor.transpose(p_t[:, k % T_RING, at:at + rows], gathered[0:rows, g % (2 * G_RING), :],
                                               identity[0:rows, 0:rows])
                    at += rows
                last.then_inc(t_done, 1)

            def interact(k):
                if k == 0:
                    pe.wait_ge(hot_copied, NH)
                    pe.wait_ge(pad_ready, 1)
                    pe.wait_ge(x_copied, 1)
                u = k // 2
                if k % 2 == 0 and u >= Z_RING:
                    pe.wait_ge(z_low_copied, u - Z_RING + 1)
                    pe.wait_ge(z_high_copied, u - Z_RING + 1)
                pe.wait_ge(t_copied, k + 1)
                w = PAIR * SLOTS
                for g in range(step_samples(k) // GROUP):
                    at = (k % 2 * (STEP_SAMPLES // GROUP) + g) * w
                    for half in range(2):
                        first = k * STEP_SAMPLES + g * GROUP + half * PAIR
                        last = nc.tensor.matmul(p_z[64 * half:64 * half + 64, u % Z_RING, at:at + w],
                                                emb[:, first:first + PAIR, :], emb[:, first:first + PAIR, 0:SLOTS],
                                                start=True, stop=True)
                if k % 2 == 1 or k == STEPS - 1:
                    last.then_inc(inter_done, 1)

            def layer1(n, c):
                if c == 0:
                    pe.wait_ge(z_low_copied, block_units(n))
                    pe.wait_ge(z_high_copied, block_units(n))
                if n == 0 and c == 0:
                    pe.wait_ge(dense_in, 16 * N_DENSE)
                    pe.wait_ge(z_pad_ready, 1)
                if n >= 1 and c % 2 == 0:
                    pe.wait_ge(h1_ready, 4 * n - 2 + c)
                at = c % 2 * BN
                for t in range(CQ):
                    last = nc.tensor.matmul(p_1[:, c // 2, at:at + BN], w1_sb[:, t, c * P:(c + 1) * P],
                                            z[:, t, n * BN:(n + 1) * BN], start=(t == 0), stop=(t == CQ - 1))
                if c % 2 == 1:
                    last.then_inc(l1_done, 1)

            def layer2(n):
                pe.wait_ge(h1_ready, 4 * (n + 1))
                if n >= 1:
                    pe.wait_ge(y_ready, n)
                for m in range(C2):
                    for c in range(C1):
                        last = nc.tensor.matmul(p_2[:, m * BN:(m + 1) * BN], w2_sb[:, c, m * P:(m + 1) * P],
                                                h1[:, c, 0:BN], start=(c == 0), stop=(c == C1 - 1))
                last.then_inc(l2_done, 1)

            def layer3(n):
                pe.wait_ge(h2_ready, n + 1)
                for c in range(C2):
                    last = nc.tensor.matmul(p_2[0:1, 0:BN], w3_sb[:, c:c + 1], h2[:, c, 0:BN],
                                            start=(c == 0), stop=(c == C2 - 1))
                last.then_inc(l3_done, 1)

            pe.wait_ge(blank_ready, 1)
            for i in range(WARM):
                nc.tensor.matmul(p_2[:], blank[:, 0:P], blank[:], start=True, stop=True)
            for what, i in ORDER:
                if what == "hot":
                    one_hot(i)
                if what == "transpose":
                    transpose(i)
                if what == "interact":
                    interact(i)
                if what == "layer1":
                    layer1(i // C1, i % C1)
                if what == "layer2":
                    layer2(i)
                if what == "layer3":
                    layer3(i)


def order():
    now = START
    done = {}
    todo = []
    next_of = dict.fromkeys(TIMES, 0)
    last = {"transpose": STEPS, "interact": STEPS, "hot": NH, "layer1": BLOCKS * C1, "layer2": BLOCKS, "layer3": BLOCKS}

    def at(what, i):
        never = float("inf")
        if what == "transpose":
            return GATHER_START + GATHER_STEP * (i + 1)
        if what == "hot":
            return START
        if what == "interact":
            return max(done.get(("transpose", min(i + 1, STEPS - 1)), never), done.get(("hot", NH - 1), never) + COPY,
                       done.get(("transpose", i), never) + COPY)
        if what == "layer1":
            return done.get(("interact", min(2 * block_units(i // C1), STEPS) - 1), never) + 2 * COPY
        if what == "layer2":
            return done.get(("layer1", C1 * i + C1 - 1), never) + 2 * COPY
        return done.get(("layer2", i), never) + 2 * COPY

    while any(next_of[w] < last[w] for w in last):
        open_work = [(w, next_of[w]) for w in TIMES if next_of[w] < last[w]]
        ready = [x for x in open_work if at(*x) <= now]
        if not ready:
            now = min(at(*x) for x in open_work)
            continue
        what, i = ready[0]
        now += TIMES[what] 
        done[what, i] = now
        next_of[what] += 1
        todo.append((what, i))
    return todo


def transposes_first(todo):
    todo = list(todo)
    for n in range(len(todo) - 1):
        if todo[n][0] == "interact" and todo[n + 1][0] == "transpose" and todo[n + 1][1] < STEPS - 1:
            todo[n], todo[n + 1] = todo[n + 1], todo[n]
    return todo


START, GATHER_START, GATHER_STEP, COPY = 6.5, 6.4, 2.08, 0.6
TIMES = {"transpose": 0.22, "interact": 0.48, "layer3": 0.5, "layer2": 1.8, "layer1": 1.5, "hot": 5.2}
ORDER = order()


def kernel(**inputs):
    import concourse.bacc as bacc
    from concourse.bass_utils import run_bass_kernel_spmd as run

    a = {name: np.asarray(v) for name, v in inputs.items()}
    ids = a["ids"]

    table = np.concatenate([a[f"tbl_{f}"] for f in GATHERED])
    padded = np.zeros((NGATHER * SG, NG), ids.dtype)
    padded[:B] = ids[:, GATHERED]
    gather_ids = padded.reshape(NGATHER, SG * NG).T
    rows = [ROWS[f] for f in GATHERED]
    first = [sum(rows[:i]) for i in range(NG)]
    gather_rows = np.array([[r - 1, s] for r, s in zip(rows, first)] * SG, np.float32)

    hot_tables = np.stack([a[f"tbl_{f}"].reshape(HP, HC * D) for f in ONEHOT])
    hot_ids = ids[:, ONEHOT].T

    x = a["r_dense_x"]
    w1 = np.zeros((4, PAD, CQ, H1), np.float32)
    x_rows = np.zeros((4, XROWS, CQ, B), np.float32)
    pair = {}
    for i in range(FEATURES + 1):
        for j in range(i + 1, FEATURES + 1):
            pair[i, j] = len(pair)
    for q in range(1, SLOTS):
        for p in range(q):
            w1[q // CQ, p, q % CQ] = a["W_top1"][pair[tuple(sorted((SLOT_FEATURE[p], SLOT_FEATURE[q])))]]
    for d in range(D):
        c, r = divmod(d, XROWS)
        w1[c // CQ, SLOTS + r, c % CQ] = a["W_top1"][len(pair) + d]
        x_rows[c // CQ, r, c % CQ] = x[:, d]

    arrays = {
        "table": table,
        "gather_ids": gather_ids,
        "gather_rows": gather_rows,
        "hot_tables": hot_tables,
        "hot_ids": hot_ids.reshape(1, NH * B),
        "x_t": x.T,
        "x_rows": x_rows,
        "w1": w1.reshape(P, CQ, H1),
        "b1": a["b_top1"].reshape(C1, P).T,
        "w2": a["W_top2"].reshape(C1, P, H2).transpose(1, 0, 2),
        "b2": a["b_top2"].reshape(C2, P).T,
        "w3": a["W_top3"].reshape(C2, P).T,
    }
    arrays = {f"in_{name}": np.ascontiguousarray(v) for name, v in arrays.items()}
    nc = bacc.Bacc("TRN2", target_bir_lowering=False, num_devices=1)
    args = {name[3:]: nc.dram_tensor(name, v.shape, mybir.dt.from_np(v.dtype), kind="ExternalInput").ap()
            for name, v in arrays.items()}
    args["hot_ids"] = args["hot_ids"].rearrange("o (e b) -> (o e) b", e=NH).partition_broadcast(HP)
    out = nc.dram_tensor("out_y", (1, B), F32, kind="ExternalOutput").ap()
    tower(nc, out=out, **args)
    result = run(nc, [arrays], core_ids=[0]).results[0]["out_y"]
    return result.reshape(B, 1)
```

```python
import numpy as np
from contextlib import ExitStack
import concourse.bass as bass
from concourse import mybir

F32 = mybir.dt.float32
BF16 = mybir.dt.bfloat16
F32R = mybir.dt.float32r
I32 = mybir.dt.int32
ALU = mybir.AluOpType
ACT = mybir.ActivationFunctionType

P = 128
B = 512
D = 128
FEATURES = 26
ROWS = [1250, 1250, 1250, 12500, 125000, 1000, 1000, 1000, 1250, 12500, 1250, 1250, 1000,
        1250, 1000, 1250, 1000, 1250, 1250, 12500, 1250, 1000, 1250, 1250, 1250, 1250]
ONEHOT = [5, 6, 7, 12, 14, 16, 21]
GATHERED = [f for f in range(FEATURES) if f not in ONEHOT]
NG, NH = len(GATHERED), len(ONEHOT)
SLOTS = NG + NH + 1
SLOT_FEATURE = GATHERED + ONEHOT + [FEATURES]
PAD = 32

HP = 125
HC = [ROWS[f] // HP for f in ONEHOT]
HC_MAX = max(HC)
CHUNKS = [(e, c) for e in range(NH) for c in range(HC[e])]
FIRST_CHUNK = [sum(HC[:e]) for e in range(NH + 1)]
HOT_PIECE = 2

NGATHER = B * NG // P
GATHERS = 4
STEP_AT = list(range(0, NGATHER - 3, GATHERS)) + [NGATHER - 2, NGATHER - 1, NGATHER]
STEPS = len(STEP_AT) - 1
GROUP = 4
PAIR = 2

HALF = SLOTS // 2
MERGED = HALF + 1
CQ = 4
H1, H2 = 512, 256
C1, C2 = H1 // P, H2 // P
BLOCK_AT = [0, 160, 288, 384, B]
BLOCKS = len(BLOCK_AT) - 1
BN = max(n - m for m, n in zip(BLOCK_AT, BLOCK_AT[1:]))
TAIL = B - BLOCK_AT[-2]
PIECE = PAD
PIECES = TAIL // PIECE

G_RING = 24
G_SEMS = 8
T_RING = 2
Z_RING = 3
WARM = 12
TABLE_RING = 3
MASK_RING = 16


def step_gathers(k):
    return range(STEP_AT[k], STEP_AT[k + 1])


def step_of(g):
    return next(k for k in range(STEPS) if g in step_gathers(k))


def gathers_counted(k):
    return sum(len(step_gathers(i)) for i in range(k % G_SEMS, k + 1, G_SEMS))


def step_groups(k):
    return range(STEP_AT[k] * P // NG // GROUP, STEP_AT[k + 1] * P // NG // GROUP)


GROUPS_MAX = max(len(step_groups(k)) for k in range(STEPS))


def block_samples(n):
    return BLOCK_AT[n + 1] - BLOCK_AT[n]


def block_steps(n):
    return next(k + 1 for k in range(STEPS) if step_groups(k).stop * GROUP >= BLOCK_AT[n + 1])


def piece_steps(i):
    return next(k + 1 for k in range(STEPS) if step_groups(k).stop * GROUP >= BLOCK_AT[-2] + (i + 1) * PIECE)


def spread_at(k):
    needed = [block_steps(n) for n in range(BLOCKS)] + [piece_steps(i) for i in range(PIECES)]
    return k % 2 == 1 and k < STEPS - 5 or k + 1 in needed


def spreads(k):
    return sum(spread_at(i) for i in range(k + 1))


def columns(j):
    return min(CQ, MERGED - j * CQ)


def tower(nc, table, gather_ids, hot_tables, hot_ids, x_t, x_rows, second, w1, w2, b2, w3, out):
    with ExitStack() as ctx:
        def sb(name, shape, dt):
            return ctx.enter_context(nc.sbuf_tensor(name, shape, dt))

        def pb(name, shape, dt):
            return ctx.enter_context(nc.psum_tensor(name, shape, dt))

        def sem(name):
            return ctx.enter_context(nc.semaphore(name))

        ids_raw = sb("ids_raw", [P, 3, NGATHER], I32)
        ids_clamped = sb("ids_clamped", [P, NGATHER], I32)
        row_ids = sb("row_ids", [P, NGATHER], I32)
        gathered = sb("gathered", [P, G_RING, D], F32)
        identity = sb("identity", [P, P], F32)
        blank = sb("blank", [P, 512], BF16)
        preload = sb("preload", [P, 1], BF16)

        hot_raw = sb("hot_raw", [HP, TABLE_RING, B], I32)
        hot_shifted = sb("hot_shifted", [HP, TABLE_RING, B], F32)
        first_row_i = sb("first_row_i", [HP, NH], I32)
        first_row = sb("first_row", [HP, NH], F32)
        tab = sb("tab", [HP, TABLE_RING, HC_MAX * D], F32)
        high = sb("high", [HP, TABLE_RING, HC_MAX * D], F32R)
        low = sb("low", [HP, TABLE_RING, HC_MAX * D], F32R)
        mask = sb("mask", [HP, MASK_RING, B], F32R)

        x_sb = sb("x_sb", [D, B], F32)
        emb = sb("emb", [D, B, PAD], F32)
        merged = sb("merged", [P, B // GROUP, PAIR, MERGED], F32)
        second_sb = sb("second_sb", [P, GROUPS_MAX, PAIR, HALF], I32)
        z = sb("z", [P, CQ, B], F32)
        w1_sb = sb("w1_sb", [P, CQ, H1], F32)
        w2_sb = sb("w2_sb", [P, C1, H2], F32)
        w3_sb = sb("w3_sb", [P, C2], F32)
        b2_sb = sb("b2_sb", [P, C2], F32)
        h1 = sb("h1", [P, C1, BN], F32)
        tail_rows = sb("tail_rows", [P, PIECES, P], F32)
        h2 = sb("h2", [P, C2, BN], F32)
        h1_tail = sb("h1_tail", [P, C1, TAIL], F32)
        h2_tail = sb("h2_tail", [P, C2, TAIL], F32)
        y = sb("y", [1, B], F32)

        p_t = pb("p_t", [P, T_RING, 512], F32)
        p_z = pb("p_z", [P, Z_RING, 512], F32)
        p_1 = pb("p_1", [P, 2, 512], F32)
        p_2 = pb("p_2", [P, 512], F32)

        ids_in = sem("ids_in")
        hot_ids_in = [sem(f"hot_ids_in{e}") for e in range(NH)]
        tab_in = [sem(f"tab_in{e}") for e in range(NH)]
        tab_half_in = sem("tab_half_in")
        x_in = sem("x_in")
        dense_in = sem("dense_in")
        blank_ready = sem("blank_ready")
        iota_done = sem("iota_done")
        zeroed = sem("zeroed")
        identity_ready = sem("identity_ready")
        ids_step = sem("ids_step")
        ids_ready = sem("ids_ready")
        gather_in = [sem(f"gather_in{i}") for i in range(G_SEMS)]
        first_row_ready = sem("first_row_ready")
        hot_ids_ready = sem("hot_ids_ready")
        mask_ready = sem("mask_ready")
        high_ready = sem("high_ready")
        low_ready = sem("low_ready")
        chunk_done = sem("chunk_done")
        hot_copied = sem("hot_copied")
        pad_ready = sem("pad_ready")
        x_copied = sem("x_copied")
        t_done = sem("t_done")
        t_copied = sem("t_copied")
        inter_done = sem("inter_done")
        first_copied = sem("first_copied")
        second_merged = sem("second_merged")
        z_low_copied = sem("z_low_copied")
        z_high_copied = sem("z_high_copied")
        l1_done = sem("l1_done")
        tail_done = sem("tail_done")
        tail_rows_ready = sem("tail_rows_ready")
        tail_turned = sem("tail_turned")
        h1_tail_ready = sem("h1_tail_ready")
        tail_l2_done = sem("tail_l2_done")
        tail_h2_ready = sem("tail_h2_ready")
        tail_l3_done = sem("tail_l3_done")
        tail_y_ready = sem("tail_y_ready")
        h1_ready = sem("h1_ready")
        l2_done = sem("l2_done")
        h2_ready = sem("h2_ready")
        l3_done = sem("l3_done")
        y_ready = sem("y_ready")
        out_done = sem("out_done")
        N_DENSE = 10

        def step_columns(k, first, end):
            count = len(step_groups(k))
            return p_z[:, k % Z_RING, 0:count * PAIR * SLOTS].rearrange("p (g s c) -> p g s c", g=count, s=PAIR)[:, :, :, first:end]

        def step_merged(k, end):
            return merged[:, step_groups(k)[0]:step_groups(k).stop, :, 0:end]

        def copy_to_z(copy, k, quadrants, signal):
            first = max([step_groups(i).stop for i in range(k) if spread_at(i)], default=0)
            end = step_groups(k).stop
            for s in quadrants:
                for j in range(4):
                    dst = z[32 * j:32 * j + SLOTS, 0:columns(j), first * GROUP:end * GROUP]
                    dst = dst.rearrange("p t (g s) -> p g t s", s=GROUP)
                    last = copy(dst[:, :, :, s], merged[32 * s:32 * s + SLOTS, first:end, s % PAIR, j * CQ:j * CQ + columns(j)])
            last.then_inc(signal, 1)

        def half(e, h):
            return slice(h * HC[e] * D // 2, (h + 1) * HC[e] * D // 2)

        p_tail = [p_1[:, 0, 0:P]] * (PIECES - 1) + [p_t[:, STEPS % T_RING, 0:P]]
        p_turned = [p_1[:, 1, 0:P]] * (PIECES - 1) + [p_t[:, (STEPS - 1) % T_RING, 0:P]]
        p_2_of = [[p_2[:, 0:BN], p_2[:, BN:2 * BN]]] * (BLOCKS - 1) + [[p_z[:, (STEPS + m) % Z_RING, :] for m in range(C2)]]
        h1_of = [h1] * (BLOCKS - 1) + [h1_tail]
        h2_of = [h2] * (BLOCKS - 1) + [h2_tail]

        block = ctx.enter_context(nc.Block())

        @block.sync
        def _(sp):
            sp.dma_start(ids_raw[:], gather_ids).then_inc(ids_in, 16)
            for e in range(NH):
                if e >= TABLE_RING:
                    sp.wait_ge(hot_ids_ready, e - TABLE_RING + 1)
                sp.dma_start(hot_raw[:, e % TABLE_RING, :], hot_ids[:, e, :]).then_inc(hot_ids_in[e], 16)
                if e == 0:
                    sp.dma_start(tab[:, 0, half(0, 1)], hot_tables[0][:, half(0, 1)]).then_inc(tab_half_in, 16)
                    continue
                if e >= TABLE_RING:
                    sp.wait_ge(low_ready, 2 * (e - TABLE_RING + 1))
                sp.dma_start(tab[:, e % TABLE_RING, 0:HC[e] * D], hot_tables[e]).then_inc(tab_in[e], 16)
            sp.dma_start(x_sb[:], x_t).then_inc(x_in, 16)
            for j in range(4):
                n = columns(j)
                sp.dma_start(z[32 * j + SLOTS:32 * j + PAD, 0:n, :], x_rows[j, SLOTS:PAD, 0:n, :]).then_inc(dense_in, 16)
            sp.dma_start(z[96:128, columns(3):CQ, :], x_rows[3, :, columns(3):CQ, :]).then_inc(dense_in, 16)
            sp.dma_start(second_sb[:], second).then_inc(dense_in, 16)
            sp.dma_start(w1_sb[:], w1).then_inc(dense_in, 16)
            sp.dma_start(w2_sb[:], w2).then_inc(dense_in, 16)
            sp.dma_start(w3_sb[:], w3).then_inc(dense_in, 16)
            sp.dma_start(b2_sb[:], b2).then_inc(dense_in, 16)
            sp.wait_ge(y_ready, BLOCKS - 1)
            sp.wait_ge(tail_y_ready, 1)
            sp.dma_start(out, y[:]).then_inc(out_done, 16)
            sp.wait_ge(out_done, 16)

        @block.gpsimd
        def _(pool):
            for n in sorted(set(HC)):
                e = HC.index(n)
                nc.gpsimd.iota(first_row_i[:, e:e + 1], [[1, 1]], base=0, channel_multiplier=-n).then_inc(iota_done, 1)
            nc.gpsimd.memset(identity[:], 0.0).then_inc(zeroed, 1)
            pool.wait_ge(zeroed, 1)
            nc.gpsimd.affine_select(out=identity[:], in_=identity[:], compare_op=ALU.not_equal, fill=1.0,
                                    base=0, pattern=[[-1, P]], channel_multiplier=1).then_inc(identity_ready, 1)
            pool.wait_ge(ids_ready, 1)
            for k in range(STEPS):
                if k >= G_SEMS:
                    pool.wait_ge(gather_in[k % G_SEMS], 16 * gathers_counted(k - G_SEMS))
                for g in step_gathers(k):
                    if g >= G_RING:
                        pool.wait_ge(t_done, step_of(g - G_RING) + 1)
                    nc.gpsimd.indirect_dma_start(
                        gathered[:, g % G_RING, :], None, table,
                        bass.IndirectOffsetOnAxis(row_ids[:, g:g + 1], 0)).then_inc(gather_in[k % G_SEMS], 16)

        @block.vector
        def _(dve):
            nc.vector.memset(blank[:], 0.0).then_inc(blank_ready, 1)
            dve.wait_ge(ids_in, 16)
            nc.vector.scalar_tensor_tensor(ids_clamped[:], ids_raw[:, 0, :], 0.0, ids_raw[:, 1, :], ALU.max, ALU.min).then_inc(ids_step, 1)
            dve.wait_ge(ids_step, 1)
            nc.vector.tensor_tensor(row_ids[:], ids_clamped[:], ids_raw[:, 2, :], ALU.add).then_inc(ids_ready, 1)
            dve.wait_ge(iota_done, len(set(HC)))
            for n in sorted(set(HC)):
                e = HC.index(n)
                nc.vector.tensor_copy(first_row[:, e:e + 1], first_row_i[:, e:e + 1]).then_inc(first_row_ready, 1)

            def make_mask(e, h):
                if h == 0:
                    dve.wait_ge(hot_ids_ready, e + 1)
                for c in range(h * HC[e] // 2, (h + 1) * HC[e] // 2):
                    m = FIRST_CHUNK[e] + c
                    if m >= MASK_RING:
                        dve.wait_ge(chunk_done, m - MASK_RING + 1)
                    nc.vector.tensor_scalar(mask[:, m % MASK_RING, :], hot_shifted[:, e % TABLE_RING, :],
                                            float(c), None, ALU.is_equal).then_inc(mask_ready, 1)

            def make_low(e, h):
                dve.wait_ge(high_ready, 2 * e + h + 1)
                if h == 0 and e >= TABLE_RING:
                    dve.wait_ge(chunk_done, FIRST_CHUNK[e - TABLE_RING + 1])
                slot = e % TABLE_RING
                nc.vector.tensor_tensor(low[:, slot, half(e, h)], tab[:, slot, half(e, h)], high[:, slot, half(e, h)],
                                        ALU.subtract).then_inc(low_ready, 1)

            for e in range(NH):
                for h in range(2):
                    make_mask(e, h)
                    make_low(e, h)
            nc.vector.memset(emb[:, :, SLOTS:PAD], 0.0).then_inc(pad_ready, 1)

            def layer1_out(n, bank):
                if n >= 1:
                    dve.wait_ge(l2_done, n)
                dve.wait_ge(l1_done, 2 * n + bank + 1)
                size = block_samples(n)
                nc.vector.tensor_scalar(h1[0:64, 2 * bank:2 * bank + 2, 0:size],
                                        p_1[0:64, bank, 0:2 * BN].rearrange("p (c n) -> p c n", c=2)[:, :, 0:size],
                                        0.0, None, ALU.max).then_inc(h1_ready, 1)

            def tail_out(i):
                dve.wait_ge(tail_done, i + 1)
                nc.vector.tensor_scalar(tail_rows[:, i, :], p_tail[i], 0.0, None, ALU.max).then_inc(tail_rows_ready, 1)

            def turned_out(i):
                dve.wait_ge(tail_turned, i + 1)
                nc.vector.tensor_copy(h1_tail[0:64, :, i * PIECE:(i + 1) * PIECE],
                                      p_turned[i][0:64].rearrange("p (c n) -> p c n", c=C1)).then_inc(h1_tail_ready, 1)

            for what, i in ORDER:
                if what == "interact":
                    if i == 0:
                        dve.wait_ge(dense_in, 16 * N_DENSE)
                    dve.wait_ge(inter_done, i + 1)
                    nc.vector.tensor_copy(step_merged(i, MERGED), step_columns(i, 0, MERGED)).then_inc(first_copied, 1)
                    dve.wait_ge(first_copied, i + 1)
                    nc.vector.copy_predicated(step_merged(i, HALF), second_sb[:, 0:len(step_groups(i))],
                                              step_columns(i, MERGED, SLOTS)).then_inc(second_merged, 1)
                    if spread_at(i):
                        dve.wait_ge(second_merged, i + 1)
                        copy_to_z(nc.vector.tensor_copy, i, (0, 1, 2), z_low_copied)
                if what == "layer1" and i % 2 == 1:
                    layer1_out(i // C1, i % C1 // 2)
                if what == "tail":
                    tail_out(i)
                if what == "turn":
                    turned_out(i)

        @block.scalar
        def _(act):
            act.dma_start(tab[:, 0, half(0, 0)], hot_tables[0][:, half(0, 0)]).then_inc(tab_in[0], 16)

            act.wait_ge(blank_ready, 1)
            nc.scalar.activation(preload[:], blank[:, 0:1], ACT.Identity)
            act.wait_ge(first_row_ready, len(set(HC)))

            def shift_ids(e):
                act.wait_ge(hot_ids_in[e], 16)
                if e >= TABLE_RING:
                    act.wait_ge(mask_ready, FIRST_CHUNK[e - TABLE_RING + 1])
                same = HC.index(HC[e])
                nc.scalar.activation(hot_shifted[:, e % TABLE_RING, :], hot_raw[:, e % TABLE_RING, :], ACT.Identity,
                                     bias=first_row[:, same:same + 1]).then_inc(hot_ids_ready, 1)

            def cut_high(e):
                act.wait_ge(tab_in[e], 16)
                if e >= TABLE_RING:
                    act.wait_ge(chunk_done, FIRST_CHUNK[e - TABLE_RING + 1])
                for h in range(2):
                    if e == 0 and h == 1:
                        act.wait_ge(tab_half_in, 16)
                    nc.scalar.copy(high[:, e % TABLE_RING, half(e, h)], tab[:, e % TABLE_RING, half(e, h)]).then_inc(high_ready, 1)

            def copy_hot(e):
                act.wait_ge(chunk_done, FIRST_CHUNK[e + 1])
                nc.scalar.copy(emb[:, :, NG + e], p_1[:, e % 2, :]).then_inc(hot_copied, 1)

            def copy_t(k):
                act.wait_ge(t_done, k + 1)
                start, stop = STEP_AT[k] * P, STEP_AT[k + 1] * P
                first, end = -(-start // NG), stop // NG
                whole = first * NG - start
                if whole:
                    nc.scalar.copy(emb[:, first - 1, NG - whole:NG], p_t[:, k % T_RING, 0:whole])
                last = nc.scalar.copy(emb[:, first:end, 0:NG], p_t[:, k % T_RING, whole:whole + (end - first) * NG]
                                      .rearrange("p (n f) -> p n f", f=NG))
                if end * NG < stop:
                    last = nc.scalar.copy(emb[:, end, 0:stop - end * NG],
                                          p_t[:, k % T_RING, end * NG - start:stop - start])
                last.then_inc(t_copied, 1)

            def layer1_out(n, bank):
                if n >= 1:
                    act.wait_ge(l2_done, n)
                act.wait_ge(l1_done, 2 * n + bank + 1)
                size = block_samples(n)
                nc.scalar.activation(h1[64:128, 2 * bank:2 * bank + 2, 0:size],
                                     p_1[64:128, bank, 0:2 * BN].rearrange("p (c n) -> p c n", c=2)[:, :, 0:size],
                                     ACT.Relu).then_inc(h1_ready, 1)

            def turned_out(i):
                act.wait_ge(tail_turned, i + 1)
                nc.scalar.copy(h1_tail[64:128, :, i * PIECE:(i + 1) * PIECE],
                               p_turned[i][64:128].rearrange("p (c n) -> p c n", c=C1)).then_inc(h1_tail_ready, 1)

            def layer2_out(n):
                act.wait_ge(l2_done, n + 1)
                if n >= 1:
                    act.wait_ge(l3_done, n)
                size = block_samples(n)
                for c in range(C2):
                    last = nc.scalar.activation(h2[:, c, 0:size], p_2_of[n][c][:, 0:size], ACT.Relu, bias=b2_sb[:, c:c + 1])
                last.then_inc(h2_ready, 1)

            def tail_layer2_out(m):
                act.wait_ge(tail_l2_done, m + 1)
                nc.scalar.activation(h2_tail[:, m, :], p_2_of[-1][m][:, 0:TAIL], ACT.Relu,
                                     bias=b2_sb[:, m:m + 1]).then_inc(tail_h2_ready, 1)

            def layer3_out(n):
                if n == BLOCKS - 1:
                    act.wait_ge(tail_l3_done, 1)
                else:
                    act.wait_ge(l3_done, n + 1)
                size = block_samples(n)
                nc.scalar.copy(y[:, BLOCK_AT[n]:BLOCK_AT[n + 1]],
                               p_2_of[n][0][0:1, 0:size]).then_inc(y_ready if n < BLOCKS - 1 else tail_y_ready, 1)

            for e in range(TABLE_RING - 1):
                shift_ids(e)
                cut_high(e)
            for what, i in COPY_ORDER:
                if what == "hot":
                    e = CHUNKS[i * HOT_PIECE][0]
                    if i * HOT_PIECE == FIRST_CHUNK[e] and e + TABLE_RING - 1 < NH:
                        shift_ids(e + TABLE_RING - 1)
                        cut_high(e + TABLE_RING - 1)
                    if (i + 1) * HOT_PIECE == FIRST_CHUNK[e + 1]:
                        copy_hot(e)
                    if i * HOT_PIECE == FIRST_CHUNK[NH - 1]:
                        act.wait_ge(x_in, 16)
                        nc.scalar.copy(emb[:, :, SLOTS - 1], x_sb[:]).then_inc(x_copied, 1)
                if what == "transpose":
                    copy_t(i)
                if what == "spread":
                    act.wait_ge(second_merged, i + 1)
                    copy_to_z(nc.scalar.copy, i, (3,), z_high_copied)
                if what == "layer1" and i % 2 == 1:
                    layer1_out(i // C1, i % C1 // 2)
                if what == "turn":
                    turned_out(i)
                if what == "layer2" and i % C2 == C2 - 1:
                    layer2_out(i // C2)
                if what == "layer3":
                    layer3_out(i)
                if what == "tail2":
                    tail_layer2_out(i)
                if what == "tail3":
                    layer3_out(BLOCKS - 1)

        @block.tensor
        def _(pe):
            def one_hot(i):
                for m in range(i * HOT_PIECE, (i + 1) * HOT_PIECE):
                    e, c = CHUNKS[m]
                    slot = e % TABLE_RING
                    if c == 0 and e >= 2:
                        pe.wait_ge(hot_copied, e - 1)
                    if c in (0, HC[e] // 2):
                        pe.wait_ge(high_ready, 2 * e + 1 + (c > 0))
                    pe.wait_ge(mask_ready, m + 1)
                    nc.tensor.matmul(p_1[:, e % 2, :], high[:, slot, c * D:(c + 1) * D], mask[:, m % MASK_RING, :],
                                     start=(c == 0), stop=False)
                    if c in (0, HC[e] // 2):
                        pe.wait_ge(low_ready, 2 * e + 1 + (c > 0))
                    last = nc.tensor.matmul(p_1[:, e % 2, :], low[:, slot, c * D:(c + 1) * D], mask[:, m % MASK_RING, :],
                                            start=False, stop=(c == HC[e] - 1))
                    last.then_inc(chunk_done, 1)

            def transpose(k):
                if k == 0:
                    pe.wait_ge(identity_ready, 1)
                pe.wait_ge(gather_in[k % G_SEMS], 16 * gathers_counted(k))
                if k >= T_RING:
                    pe.wait_ge(t_copied, k - T_RING + 1)
                for i, g in enumerate(step_gathers(k)):
                    last = nc.tensor.transpose(p_t[:, k % T_RING, i * P:(i + 1) * P], gathered[:, g % G_RING, :], identity[:])
                last.then_inc(t_done, 1)

            def interact(k):
                if k == 0:
                    pe.wait_ge(hot_copied, NH)
                    pe.wait_ge(pad_ready, 1)
                    pe.wait_ge(x_copied, 1)
                if k >= Z_RING:
                    pe.wait_ge(second_merged, k - Z_RING + 1)
                pe.wait_ge(t_copied, k + 1)
                w = PAIR * SLOTS
                for i, g in enumerate(step_groups(k)):
                    for half in range(2):
                        first = g * GROUP + half * PAIR
                        last = nc.tensor.matmul(p_z[64 * half:64 * half + 64, k % Z_RING, i * w:(i + 1) * w],
                                                emb[:, first:first + PAIR, :], emb[:, first:first + PAIR, 0:SLOTS],
                                                start=True, stop=True)
                last.then_inc(inter_done, 1)

            def layer1(n, c):
                if c == 0:
                    pe.wait_ge(z_low_copied, spreads(block_steps(n) - 1))
                    pe.wait_ge(z_high_copied, spreads(block_steps(n) - 1))
                if n == 0 and c == 0:
                    pe.wait_ge(dense_in, 16 * N_DENSE)
                if n >= 1 and c % 2 == 0:
                    pe.wait_ge(h1_ready, 4 * n - 2 + c)
                at = c % 2 * BN
                for t in range(CQ):
                    last = nc.tensor.matmul(p_1[:, c // 2, at:at + block_samples(n)], w1_sb[:, t, c * P:(c + 1) * P],
                                            z[:, t, BLOCK_AT[n]:BLOCK_AT[n + 1]], start=(t == 0), stop=(t == CQ - 1))
                if c % 2 == 1:
                    last.then_inc(l1_done, 1)

            def tail(i):
                first = BLOCK_AT[-2] + i * PIECE
                pe.wait_ge(z_low_copied, spreads(piece_steps(i) - 1))
                pe.wait_ge(z_high_copied, spreads(piece_steps(i) - 1))
                if i == 0:
                    pe.wait_ge(h1_ready, 4 * (BLOCKS - 1))
                elif i < PIECES - 1:
                    pe.wait_ge(tail_rows_ready, i)
                else:
                    pe.wait_ge(t_copied, STEPS - 1)
                for t in range(CQ):
                    for c in range(C1):
                        last = nc.tensor.matmul(p_tail[i][32 * c:32 * c + PIECE, :], z[:, t, first:first + PIECE],
                                                w1_sb[:, t, c * P:(c + 1) * P], start=(t == 0), stop=(t == CQ - 1))
                last.then_inc(tail_done, 1)

            def turn(i):
                pe.wait_ge(tail_rows_ready, i + 1)
                if i == PIECES - 1:
                    pe.wait_ge(t_copied, STEPS)
                elif i > 0:
                    pe.wait_ge(h1_tail_ready, 2 * i)
                nc.tensor.transpose(p_turned[i], tail_rows[:, i, :], identity[:]).then_inc(tail_turned, 1)

            def layer2(n, m):
                if m == 0 and n < BLOCKS - 1:
                    pe.wait_ge(h1_ready, 4 * (n + 1))
                if m == 0 and 1 <= n < BLOCKS - 1:
                    pe.wait_ge(y_ready, n)
                if m == 0 and n == BLOCKS - 1:
                    pe.wait_ge(h1_tail_ready, 2 * PIECES)
                if n == BLOCKS - 1:
                    pe.wait_ge(second_merged, STEPS - Z_RING + 1 + m)
                size = block_samples(n)
                for c in range(C1):
                    last = nc.tensor.matmul(p_2_of[n][m][:, 0:size], w2_sb[:, c, m * P:(m + 1) * P],
                                            h1_of[n][:, c, 0:size], start=(c == 0), stop=(c == C1 - 1))
                if n == BLOCKS - 1:
                    last.then_inc(tail_l2_done, 1)
                elif m == C2 - 1:
                    last.then_inc(l2_done, 1)

            def layer3(n):
                size = block_samples(n)
                if n < BLOCKS - 1:
                    pe.wait_ge(h2_ready, n + 1)
                for c in range(C2):
                    if n == BLOCKS - 1:
                        pe.wait_ge(tail_h2_ready, c + 1)
                    last = nc.tensor.matmul(p_2_of[n][0][0:1, 0:size], w3_sb[:, c:c + 1], h2_of[n][:, c, 0:size],
                                            start=(c == 0), stop=(c == C2 - 1))
                last.then_inc(l3_done if n < BLOCKS - 1 else tail_l3_done, 1)

            def fill(k, n):
                if k >= Z_RING:
                    pe.wait_ge(second_merged, k - Z_RING + 1)
                for i in range(n):
                    nc.tensor.matmul(p_z[:, k % Z_RING, :], blank[:, 0:P], blank[:], start=True, stop=True)

            pe.wait_ge(blank_ready, 1)
            for i in range(WARM):
                nc.tensor.matmul(p_2[:], blank[:, 0:P], blank[:], start=True, stop=True)
            for what, i in ORDER:
                if what == "hot":
                    one_hot(i)
                if what == "transpose":
                    transpose(i)
                if what == "interact":
                    interact(i)
                if what == "layer1":
                    layer1(i // C1, i % C1)
                if what == "tail":
                    tail(i)
                if what == "turn":
                    turn(i)
                if what == "layer2":
                    layer2(i // C2, i % C2)
                if what == "layer3":
                    layer3(i)
                if what == "tail2":
                    layer2(BLOCKS - 1, i)
                if what == "tail3":
                    layer3(BLOCKS - 1)
                if what == "fill":
                    fill(*i)


def order():
    now = START
    done = {}
    work = []
    next_of = dict.fromkeys(TIMES, 0)
    count = {"transpose": STEPS, "interact": STEPS, "hot": len(CHUNKS) // HOT_PIECE, "layer1": (BLOCKS - 1) * C1,
             "layer2": (BLOCKS - 1) * C2, "layer3": BLOCKS - 1}
    for what, i in END:
        count[what] = min(count[what], i) if what in count else 0

    def at(what, i):
        def end(*piece):
            return done.get(piece, float("inf"))

        if what == "transpose":
            slack = HOT_SLACK if next_of["hot"] < count["hot"] else 0
            return max(GATHER_START + GATHER_STEP * STEP_AT[i + 1] + slack, FIRST_GATHER)
        if what == "hot":
            return HOT_START + HOT_STEP * (i + 1)
        if what == "interact":
            at_once = i + 1 in [block_steps(n) for n in range(BLOCKS)] or i >= STEPS - AT_ONCE
            return max(end("transpose", i) + COPY, end("hot", count["hot"] - 1) + COPY, end("transpose", i + 1 - at_once))
        if what == "layer1":
            return end("interact", block_steps(i // C1) - 1) + MERGE[i // C1]
        if what == "layer2":
            n = i // C2
            return max(end("layer1", C1 * n + C1 - 1), end("layer3", n - 1) if n > 0 else 0) + 1.5 * COPY
        return end("layer2", C2 * i + C2 - 1) + 1.5 * COPY

    while any(next_of[w] < count[w] for w in TIMES):
        open_work = [(w, next_of[w]) for w in TIMES if next_of[w] < count[w]]
        ready = [x for x in open_work if at(*x) <= now]
        if not ready:
            after = min(at(*x) for x in open_work)
            n = int((after - now) / FILL)
            if n >= FILL_LEAST and next_of["interact"] < STEPS:
                work.append((now, "fill", (next_of["interact"], n)))
            now = after
            continue
        what, i = ready[1 if len(ready) > 1 and work[-1][1] == "transpose" == ready[0][0] else 0]
        time = TIMES[what]
        if what in ("layer1", "layer2"):
            time *= max(block_samples(i // (C1 if what == "layer1" else C2)) / P, 1)
        if what == "interact":
            time *= len(step_groups(i)) / GROUPS_MAX
        if what == "transpose":
            time *= len(step_gathers(i)) / GATHERS
        now += time
        done[what, i] = now
        next_of[what] += 1
        work.append((now, what, i))
    for what, i in END:
        now += TIMES_END[what]
        work.append((now, what, i))
    return work


START, FIRST_GATHER, GATHER_START, GATHER_STEP, COPY = 5.879, 12.0, 5.7, 1.037, 0.78
HOT_START, HOT_STEP, SPREAD, HOT_SLACK, AT_ONCE = 6.682, 0.98, 0.75, 2.0, 9
FILL, FILL_LEAST = 0.312, 3
MERGE = [3.26, 1.44, 2.1]
TIMES = {"transpose": 0.43, "interact": 1.1, "layer2": 0.87, "layer3": 0.4, "layer1": 0.86, "hot": 0.86}
END = [("transpose", STEPS - 5), ("layer2", C2 * (BLOCKS - 2)), ("interact", STEPS - 5), ("tail", 0),
       ("transpose", STEPS - 4), ("layer2", C2 * (BLOCKS - 2) + 1), ("turn", 0), ("interact", STEPS - 4),
       ("transpose", STEPS - 3), ("transpose", STEPS - 2), ("tail", 1), ("transpose", STEPS - 1),
       ("interact", STEPS - 3), ("interact", STEPS - 2), ("interact", STEPS - 1), ("tail", 2),
       ("layer3", BLOCKS - 2), ("turn", 1), ("tail", 3), ("turn", 2), ("turn", 3), ("tail2", 0), ("tail2", 1),
       ("tail3", 0)]
TIMES_END = {"transpose": 0.15, "interact": 0.35, "tail": 1.2, "turn": 0.2, "layer1": 0.87, "layer2": 0.87, "layer3": 0.4,
             "tail2": 0.8, "tail3": 0.5}
WORK = order()
ORDER = [(what, i) for _, what, i in WORK]
SPREADS = [(now + SPREAD, "spread", i) for now, what, i in WORK if what == "interact" and spread_at(i)]
COPY_ORDER = [(what, i) for _, what, i in sorted(WORK + SPREADS, key=lambda x: x[0])]


def kernel(**inputs):
    import concourse.bacc as bacc
    from concourse.bass_utils import run_bass_kernel_spmd as run

    a = {name: np.asarray(v) for name, v in inputs.items()}
    ids = a["ids"]

    table = np.concatenate([a[f"tbl_{f}"] for f in GATHERED])
    rows = [ROWS[f] for f in GATHERED]
    first = np.array([sum(rows[:i]) for i in range(NG)], ids.dtype)
    kinds = (ids[:, GATHERED], np.array(rows, ids.dtype) - 1, first)
    gather_ids = np.stack([np.broadcast_to(v, (B, NG)).reshape(NGATHER, P).T for v in kinds], axis=1)

    hot_ids = ids[:, ONEHOT].T

    x = a["r_dense_x"]
    w1 = np.zeros((4, PAD, CQ, H1), np.float32)
    x_rows = np.zeros((4, PAD, CQ, B), np.float32)
    second = np.zeros((4, PAD, GROUPS_MAX, PAIR, HALF), np.int32)
    pair = {}
    for i in range(FEATURES + 1):
        for j in range(i + 1, FEATURES + 1):
            pair[i, j] = len(pair)
    for q in range(SLOTS):
        for p in [r % SLOTS for r in range(q + 1, q + HALF + 1)]:
            j, t = divmod(q % MERGED, CQ)
            w1[j, p, t] = a["W_top1"][pair[tuple(sorted((SLOT_FEATURE[p], SLOT_FEATURE[q])))]]
            if q >= MERGED:
                second[:, p, :, :, q - MERGED] = 1
    left = [(j, r, t) for j in range(4) for t in range(CQ) for r in range(SLOTS if t < columns(j) else 0, PAD)]
    for d, at in enumerate(left[:D]):
        w1[at] = a["W_top1"][len(pair) + d]
        x_rows[at] = x[:, d]
    w1[left[D]] = a["b_top1"]
    x_rows[left[D]] = 1

    arrays = {
        "table": table,
        "gather_ids": gather_ids,
        **{f"hot_table{e}": a[f"tbl_{f}"].reshape(HP, HC[e] * D) for e, f in enumerate(ONEHOT)},
        "hot_ids": hot_ids.reshape(1, NH * B),
        "x_t": x.T,
        "x_rows": x_rows,
        "second": second.reshape(P, GROUPS_MAX, PAIR, HALF),
        "w1": w1.reshape(P, CQ, H1),
        "w2": a["W_top2"].reshape(C1, P, H2).transpose(1, 0, 2),
        "b2": a["b_top2"].reshape(C2, P).T,
        "w3": a["W_top3"].reshape(C2, P).T,
    }
    arrays = {f"in_{name}": np.ascontiguousarray(v) for name, v in arrays.items()}
    nc = bacc.Bacc("TRN2", target_bir_lowering=False, num_devices=1)
    args = {name[3:]: nc.dram_tensor(name, v.shape, mybir.dt.from_np(v.dtype), kind="ExternalInput").ap()
            for name, v in arrays.items()}
    args["hot_ids"] = args["hot_ids"].rearrange("o (e b) -> (o e) b", e=NH).partition_broadcast(HP)
    args["hot_tables"] = [args.pop(f"hot_table{e}") for e in range(NH)]
    out = nc.dram_tensor("out_y", (1, B), F32, kind="ExternalOutput").ap()
    tower(nc, out=out, **args)
    result = run(nc, [arrays], core_ids=[0]).results[0]["out_y"]
    return result.reshape(B, 1)
```
